# Optimizing a Trainium2 kernel written in Bass

```python
import numpy as np
import jax
import jax.numpy as jnp

def _softmax(x, axis=-1):
    return jax.nn.softmax(x, axis=axis)

def _gelu(x):
    return jax.nn.gelu(x, approximate=True)

def _silu(x):
    return jax.nn.silu(x)

def _sigmoid(x):
    return jax.nn.sigmoid(x)

def _layernorm(x, axis=-1, eps=1e-05):
    m = jnp.mean(x, axis=axis, keepdims=True)
    v = jnp.var(x, axis=axis, keepdims=True)
    return (x - m) / jnp.sqrt(v + eps)

def _scatter_add(tgt, idx, src, axis=0):
    return tgt.at[idx].add(src)

def _segment_sum(src, seg, n):
    return jax.ops.segment_sum(src, seg, n)
kernel_name = 'mk_adj_preln_d1_adj_r2_30c0c3'

def setup_inputs(seed: int=0):
    np.random.seed(seed)
    _w = jnp.asarray

    def _rec_inputs():
        import jax
        import jax.numpy as jnp
        _gk = jax.random.key(seed)
        x = -0.0002422 + 1 * jax.random.normal(jax.random.fold_in(_gk, 1), (8, 1024, 128), jnp.float32)
        _a = jax.random.bernoulli(jax.random.fold_in(_gk, 2), 0.00195312, (8, 1024, 1024))
        adj = _a.astype(jnp.int32)
        return (x, adj)
    x, adj = _rec_inputs()

    def _L0_gnn_setup():
        import jax, jax.numpy as jnp
        import numpy as np
        NEG_INF = -9000000000000000.0
        LEAKY_SLOPE = 0.2
        key = jax.random.key(seed)
        k1, k2, k3, k4, k5, k6 = jax.random.split(key, 6)
        B, N, D = (256, 200, 128)
        hidden = jax.random.normal(k1, (B, N, D), dtype=jnp.float32)
        adj = jax.random.randint(k2, (B, N, N), 0, 5, dtype=jnp.int32)
        a0 = jax.random.normal(k3, (D,), dtype=jnp.float32)
        a1 = jax.random.normal(k4, (D,), dtype=jnp.float32)
        a2 = jax.random.normal(k5, (D,), dtype=jnp.float32)
        a3 = jax.random.normal(k6, (D,), dtype=jnp.float32)
        return {'hidden': hidden, 'adj': adj, 'a0': a0, 'a1': a1, 'a2': a2, 'a3': a3}
    _L0_gnn_all = _L0_gnn_setup()
    _L0_gnn_in = {k: v for k, v in _L0_gnn_all.items() if k in ('a0', 'a1', 'a2', 'a3')}
    del _L0_gnn_all
    return {'x': x, 'adj': adj, 'L0_gnn_a0': _L0_gnn_in['a0'], 'L0_gnn_a1': _L0_gnn_in['a1'], 'L0_gnn_a2': _L0_gnn_in['a2'], 'L0_gnn_a3': _L0_gnn_in['a3']}

def reference(x, adj, L0_gnn_a0, L0_gnn_a1, L0_gnn_a2, L0_gnn_a3):
    import jax
    import jax.numpy as jnp

    def _L0_gnn_ref(hidden, adj, a0, a1, a2, a3):
        import jax, jax.numpy as jnp
        import numpy as np
        NEG_INF = -9000000000000000.0
        LEAKY_SLOPE = 0.2

        def edge_score(a):
            s = jnp.einsum('bid,bjd->bij', hidden * a, hidden)
            return jax.nn.leaky_relu(s, LEAKY_SLOPE)
        e0, e1, e2, e3 = (edge_score(a0), edge_score(a1), edge_score(a2), edge_score(a3))
        alpha = jnp.where(adj == 1, e0, NEG_INF)
        alpha = jnp.where(adj == 2, e1, alpha)
        alpha = jnp.where(adj == 3, e2, alpha)
        alpha = jnp.where(adj == 4, e3, alpha)
        alpha = jax.nn.softmax(alpha, axis=-1)
        return jnp.matmul(alpha, hidden)
    h = jnp.maximum(_layernorm(x, axis=-1), 0.0)
    x = x + _L0_gnn_ref(h, adj, L0_gnn_a0, L0_gnn_a1, L0_gnn_a2, L0_gnn_a3)
    return x

_drawn_inputs = setup_inputs


def setup_inputs(seed=0):
    import zlib

    import numpy as np

    out = dict(_drawn_inputs(seed))
    spreads = {}
    factors = {}
    for name, (base, spread) in spreads.items():
        noise = np.random.default_rng([zlib.crc32(name.encode()), seed]).standard_normal(out[name].shape)
        drawn = base * np.exp(spread * noise) if base else spread * noise
        out[name] = jnp.asarray(drawn.astype(out[name].dtype))
    for name, factor in factors.items():
        out[name] = (out[name] * factor).astype(out[name].dtype)
    return out
```

```python
from contextlib import ExitStack

import concourse.bass as bass
from concourse import mybir

F32 = mybir.dt.float32
BF16 = mybir.dt.bfloat16
I32 = mybir.dt.int32
U32 = mybir.dt.uint32
ALU = mybir.AluOpType
ACT = mybir.ActivationFunctionType
AX_X = mybir.AxisListType.X

P = 128
SLOPE = 0.2
EPS = 1e-5
BIG = 2.0 ** 90
FLAG_BELOW = -(2.0 ** 80)


def build(nc, x, adj, a0, a1, a2, a3, out):
    B, N, D = x.shape
    T = N // P
    BPI = 2
    K = BPI * T
    ITERS = B // BPI
    assert D == P and N == 1024 and B % BPI == 0
    HALF = N // 2
    ADJ_SLOTS = 4
    MASK_SLOTS = 4
    STORE = 4
    OUT_SLOTS = K // STORE
    STATS_STEPS, NORM_STEP, TURN_STEPS = (1, 2), 3, (4, 5)

    ctx = ExitStack()
    with ctx:
        def sb(name, shape, dt=F32):
            return ctx.enter_context(nc.sbuf_tensor(name, shape, dt))

        def ps(name, shape, dt=F32):
            return ctx.enter_context(nc.psum_tensor(name, shape, dt))

        def sem(name):
            return ctx.enter_context(nc.semaphore(name))

        ident = sb("ident", [P, P])
        neg_half = sb("neg_half", [P, T])
        a_col = sb("a_col", [P, 4])
        neg_a = sb("neg_a", [P, 4])
        x_sb = sb("x_sb", [P, 2, T, D])
        h_sb = sb("h_sb", [P, 2, T, D])
        hT = sb("hT", [P, 2, N])
        haT = sb("haT", [P, 4, N])
        stats = sb("stats", [P, T, 6])
        mv = sb("mv", [P, T, 2])
        neg_mean = sb("neg_mean", [P, T])
        var_eps = sb("var_eps", [P, T])
        rstd = sb("rstd", [P, T])
        adj_sb = sb("adj_sb", [P, ADJ_SLOTS, 2, N], I32)
        mask = sb("mask", [P, MASK_SLOTS, N], BF16)
        masked = sb("masked", [P, N])
        leaky = sb("leaky", [P, 2, N])
        prob = sb("prob", [P, 2, N])
        probT = sb("probT", [P, N])
        neg_max = sb("neg_max", [P, K])
        bias = sb("bias", [P, K])
        row_sum = sb("row_sum", [P, K])
        inv_sum = sb("inv_sum", [P, K])
        least = sb("least", [P, K])
        lane_least = sb("lane_least", [P, 1])
        all_least = sb("all_least", [1, 1])
        hit = sb("hit", [P, N], I32)
        flag = sb("flag", [1, 1], I32)
        o_sb = sb("o_sb", [P, OUT_SLOTS, STORE, D])

        scores = ps("scores", [P, 2, N])
        pT = ps("pT", [P, 2, HALF])
        agg = ps("agg", [P, D])
        turn = ps("turn", [P, HALF])

        a_loaded = sem("a_loaded")
        waits_taken = sem("waits_taken")
        x_loaded = [sem(f"x_loaded{i}") for i in range(2)]
        adj_loaded = [sem(f"adj_loaded{i}") for i in range(ADJ_SLOTS)]
        zeroed = sem("zeroed")
        ident_ready = sem("ident_ready")
        neg_a_ready = sem("neg_a_ready")
        stats_ready = sem("stats_ready")
        mv_ready = sem("mv_ready")
        moments_ready = sem("moments_ready")
        rstd_ready = sem("rstd_ready")
        normed = sem("normed")
        h_ready = sem("h_ready")
        turned = sem("turned")
        hT_ready = sem("hT_ready")
        haT_ready = sem("haT_ready")
        mask_ready = sem("mask_ready")
        scores_ready = sem("scores_ready")
        masked_ready = sem("masked_ready")
        bias_ready = sem("bias_ready")
        leaky_ready = sem("leaky_ready")
        prob_ready = sem("prob_ready")
        pT_ready = sem("pT_ready")
        probT_ready = sem("probT_ready")
        agg_ready = sem("agg_ready")
        inv_ready = sem("inv_ready")
        o_ready = sem("o_ready")
        least_ready = sem("least_ready")
        lane_least_ready = sem("lane_least_ready")
        lanes_turned = sem("lanes_turned")
        all_least_ready = sem("all_least_ready")
        hit_ready = sem("hit_ready")
        picked0 = sem("picked0")
        picked = sem("picked")
        compared = sem("compared")
        least_of_row = sem("least_of_row")
        flag_ready = sem("flag_ready")
        stored = [sem(f"stored{i}") for i in range(OUT_SLOTS)]

        x_v = x.rearrange("b (t p) d -> b p t d", p=P)
        out_v = out.rearrange("b (t p) d -> b p t d", p=P)
        adj_v = adj.rearrange("b (t p) n -> b p t n", p=P)

        def stand_alone(eng):
            eng.sem_inc(waits_taken, 1)

        with nc.Block() as block:

            @block.sync
            def _(eng):
                def load_x(b, slot):
                    eng.dma_start(x_sb[:, slot], x_v[b]).then_inc(x_loaded[slot], 16)

                def load_adj(b, t):
                    slot = t // 2 % ADJ_SLOTS
                    eng.dma_start(adj_sb[:, slot], adj_v[b, :, t:t + 2, :]).then_inc(adj_loaded[slot], 16)

                def store(b, q, slot, done):
                    eng.wait_ge(o_ready, done + 1)
                    eng.dma_start(out_v[b, :, STORE * q:STORE * (q + 1), :],
                                  o_sb[:, slot]).then_inc(stored[slot], 16)

                def store_of(it, q):
                    store(it * BPI + q * STORE // T, q % (T // STORE), q, it * K + (q + 1) * STORE)

                def body(it, last):
                    for k in range(0, K, 2):
                        if k % T == 0 and not (last and k):
                            eng.wait_ge(o_ready, it * K + k + 1)
                            load_x(it * BPI + k // T + 1, (k // T + 1) % 2)
                        ahead = k + 2 * ADJ_SLOTS
                        if not (last and ahead >= K):
                            eng.wait_ge(mask_ready, it * K + k + 2)
                            load_adj(it * BPI + ahead // T, ahead % T)
                        if k and k % STORE == 0:
                            store_of(it, k // STORE - 1)
                    store_of(it, OUT_SLOTS - 1)

                for s in stored:
                    eng.sem_inc(s, 1)
                load_x(0, 0)
                for i, a in enumerate((a0, a1, a2, a3)):
                    eng.dma_start(a_col[:, i:i + 1], a.rearrange("(d o) -> d o", o=1)).then_inc(a_loaded, 16)
                for s in range(ADJ_SLOTS):
                    load_adj(0, 2 * s)
                with eng.Fori(0, ITERS - 1) as it:
                    body(it, False)
                body(ITERS - 1, True)
                for s in stored:
                    eng.wait_ge(s, 16 * ITERS + 1)

                eng.wait_ge(flag_ready, 1)
                with eng.If(eng.value_load(flag[0:1, 0:1]) != 0):
                    with eng.Fori(0, B) as b:
                        eng.wait_ge(o_ready, (b + B) * T + 1)
                        load_x(b, 0)
                        eng.wait_ge(compared, b * T + 1)
                        for s in range(ADJ_SLOTS):
                            load_adj(b, 2 * s)
                        for q in range(T // STORE):
                            store(b, q, q, (b + B) * T + (q + 1) * STORE)
                    for q in range(T // STORE):
                        eng.wait_ge(stored[q], 16 * (ITERS + B) + 1)

            @block.gpsimd
            def _(eng):
                def convert(loads, k):
                    eng.wait_ge(adj_loaded[k // 2 % ADJ_SLOTS], 16 * loads)
                    stand_alone(eng)
                    eng.tensor_scalar(mask[:, k % MASK_SLOTS], adj_sb[:, k // 2 % ADJ_SLOTS, k % 2].bitcast(U32),
                                      -BIG, BIG, ALU.mult, ALU.add).then_inc(mask_ready, 1)

                def normalise(c, slot):
                    eng.wait_ge(mv_ready, (c + 1) * T)
                    stand_alone(eng)
                    eng.tensor_scalar(neg_mean[:, :], mv[:, :, 0], -1.0, 0.0, ALU.mult, ALU.add).then_inc(moments_ready, 1)
                    eng.tensor_scalar(var_eps[:, :], mv[:, :, 1], EPS, 1.0, ALU.add, ALU.mult).then_inc(moments_ready, 1)
                    eng.wait_ge(moments_ready, 2 * c + 2)
                    eng.tensor_tensor(rstd[:, :], var_eps[:, :], neg_half[:, :], ALU.pow).then_inc(rstd_ready, 1)
                    eng.wait_ge(rstd_ready, c + 1)
                    stand_alone(eng)
                    for t in range(T):
                        eng.tensor_scalar(h_sb[:, slot, t], x_sb[:, slot, t], neg_mean[:, t:t + 1], rstd[:, t:t + 1],
                                          ALU.add, ALU.mult).then_inc(normed, 1)
                    eng.wait_ge(normed, (c + 1) * T)
                    stand_alone(eng)
                    eng.tensor_scalar(h_sb[:, slot], h_sb[:, slot], 3.0e38, 0.0, ALU.min, ALU.max).then_inc(h_ready, 1)

                def body(it, last):
                    for k in range(K):
                        ahead = k + MASK_SLOTS
                        if not (last and ahead >= K):
                            eng.wait_ge(masked_ready, it * K + k + 1)
                            convert(it * (K // 2 // ADJ_SLOTS) + ahead // 2 // ADJ_SLOTS + 1, ahead)
                        if k % T == NORM_STEP and not (last and k > T):
                            c = it * BPI + k // T + 1
                            eng.wait_ge(agg_ready, (c - 1) * T + 1)
                            normalise(c, (k // T + 1) % 2)

                eng.memset(ident[:, :], 0.0).then_inc(zeroed, 1)
                eng.memset(neg_half[:, :], -0.5).then_inc(zeroed, 1)
                eng.wait_ge(zeroed, 2)
                eng.affine_select(out=ident[:, :], in_=ident[:, :], compare_op=ALU.not_equal, fill=1.0,
                                  base=0, pattern=[[-1, P]], channel_multiplier=1).then_inc(ident_ready, 1)
                normalise(0, 0)
                for k in range(MASK_SLOTS):
                    convert(1, k)
                with eng.Fori(0, ITERS - 1) as it:
                    body(it, False)
                body(ITERS - 1, True)

                eng.wait_ge(flag_ready, 1)
                with eng.If(eng.value_load(flag[0:1, 0:1]) != 0):
                    with eng.Fori(0, B) as b:
                        eng.wait_ge(agg_ready, (b + B) * T + 1)
                        normalise(b + B, 0)

            @block.tensor
            def _(eng):
                def turn_h(c, slot, half):
                    eng.wait_ge(h_ready, c + 1)
                    eng.wait_ge(hT_ready, 2 * c + half)
                    for j in range(T // 2):
                        ins = eng.transpose(turn[:, j * P:(j + 1) * P], h_sb[:, slot, half * T // 2 + j], ident[:, :])
                    ins.then_inc(turned, 1)

                def score(bank, slot, t, which):
                    for j in range(2):
                        ins = eng.matmul(scores[:, bank, j * HALF:(j + 1) * HALF], haT[:, which, t * P:(t + 1) * P],
                                         hT[:, slot, j * HALF:(j + 1) * HALF], start=True, stop=True)
                    ins.then_inc(scores_ready, 1)

                def score_tile(it, k):
                    if k % T == 0:
                        eng.wait_ge(hT_ready, 2 * (it * BPI + k // T) + 2)
                        eng.wait_ge(haT_ready, 2 * (it * BPI + k // T) + 2)
                    if k >= 2:
                        eng.wait_ge(masked_ready, it * K + k - 1)
                    score(k % 2, k // T % 2, k % T, k // T % 2)

                def turn_prob(g, src):
                    eng.wait_ge(prob_ready, g + 1)
                    for j in range(2):
                        for i in range(T // 2):
                            b = j * T // 2 + i
                            ins = eng.transpose(pT[:, j, i * P:(i + 1) * P], prob[:, src, b * P:(b + 1) * P], ident[:, :])
                        ins.then_inc(pT_ready, 1)

                def aggregate(g, slot):
                    eng.wait_ge(o_ready, g + 1)
                    for b in range(T):
                        if b % (T // 2) == 0:
                            eng.wait_ge(probT_ready, g * 2 + 1 + b // (T // 2))
                        ins = eng.matmul(agg[:, :], probT[:, b * P:(b + 1) * P], h_sb[:, slot, b],
                                         start=(b == 0), stop=(b == T - 1))
                    ins.then_inc(agg_ready, 1)

                def body(it, last):
                    for k in range(K):
                        turn_prob(it * K + k, k % 2)
                        if not (last and k + 2 >= K):
                            score_tile(it, k + 2)
                        aggregate(it * K + k, k // T)
                        if k % T in TURN_STEPS and not (last and k > T):
                            turn_h(it * BPI + k // T + 1, (k // T + 1) % 2, TURN_STEPS.index(k % T))

                eng.sem_inc(agg_ready, 1)
                eng.wait_ge(ident_ready, 1)
                for half in range(2):
                    turn_h(0, 0, half)
                score_tile(0, 0)
                score_tile(0, 1)
                with eng.Fori(0, ITERS - 1) as it:
                    body(it, False)
                body(ITERS - 1, True)

                eng.wait_ge(lane_least_ready, 1)
                eng.transpose(turn[0:1, 0:P], lane_least[:, :], ident[:, :]).then_inc(lanes_turned, 1)

                eng.wait_ge(flag_ready, 1)
                with eng.If(eng.value_load(flag[0:1, 0:1]) != 0):
                    with eng.Fori(0, B) as b:
                        for half in range(2):
                            turn_h(b + B, 0, half)
                        eng.wait_ge(hT_ready, 2 * (b + B) + 2)
                        eng.wait_ge(haT_ready, 2 * (b + B) + 2)
                        for t in range(T):
                            for a in range(4):
                                if a >= 2:
                                    eng.wait_ge(picked, 4 * (b * T + t) + a - 1)
                                score(a % 2, 0, t, a)
                            turn_prob((b + B) * T + t, 0)
                            aggregate((b + B) * T + t, 0)

            @block.scalar
            def _(eng):
                def copy_probT(g):
                    for j in range(2):
                        eng.wait_ge(pT_ready, g * 2 + j + 1)
                        nc.scalar.copy(probT[:, j * HALF:(j + 1) * HALF], pT[:, j]).then_inc(probT_ready, 1)

                def exponential(g, slot, col):
                    eng.wait_ge(leaky_ready, g + 1)
                    nc.scalar.activation(prob[:, slot], leaky[:, slot], ACT.Exp, bias=bias[:, col:col + 1], scale=-1.0,
                                         accum_out=row_sum[:, col:col + 1]).then_inc(prob_ready, 1)

                def copy_hT(c, slot, half):
                    eng.wait_ge(turned, c * 2 + half + 1)
                    nc.scalar.copy(hT[:, slot, half * HALF:(half + 1) * HALF], turn[:, :]).then_inc(hT_ready, 1)

                def body(it, last):
                    for k in range(K):
                        copy_probT(it * K + k)
                        if not (last and k + 1 >= K):
                            exponential(it * K + k + 1, (k + 1) % 2, (k + 1) % K)
                        if k % T in TURN_STEPS and not (last and k > T):
                            copy_hT(it * BPI + k // T + 1, (k // T + 1) % 2, TURN_STEPS.index(k % T))

                for half in range(2):
                    copy_hT(0, 0, half)
                exponential(0, 0, 0)
                with eng.Fori(0, ITERS - 1) as it:
                    body(it, False)
                body(ITERS - 1, True)

                eng.wait_ge(flag_ready, 1)
                with eng.If(eng.value_load(flag[0:1, 0:1]) != 0):
                    with eng.Fori(0, B) as b:
                        for half in range(2):
                            copy_hT(b + B, 0, half)
                        for t in range(T):
                            exponential((b + B) * T + t, 0, t)
                            copy_probT((b + B) * T + t)

            @block.vector
            def _(eng):
                def moments(c, slot, tiles):
                    for t in tiles:
                        eng.bn_stats(stats[:, t], x_sb[:, slot, t]).then_inc(stats_ready, 1)
                    eng.wait_ge(stats_ready, c * T + tiles[-1] + 1)
                    stand_alone(eng)
                    for t in tiles:
                        eng.bn_aggr(mv[:, t], stats[:, t]).then_inc(mv_ready, 1)

                def scale_hT(c, src, half, slots):
                    eng.wait_ge(hT_ready, c * 2 + half + 1)
                    for slot, a in slots:
                        ins = eng.tensor_scalar(haT[:, slot, half * HALF:(half + 1) * HALF],
                                                hT[:, src, half * HALF:(half + 1) * HALF],
                                                neg_a[:, a:a + 1], None, ALU.mult)
                    ins.then_inc(haT_ready, 1)

                def leaky_relu(g, slot, col):
                    eng.scalar_tensor_tensor(bias[:, col:col + 1], neg_max[:, col:col + 1], SLOPE, neg_max[:, col:col + 1],
                                             op0=ALU.mult, op1=ALU.min).then_inc(bias_ready, 1)
                    eng.scalar_tensor_tensor(leaky[:, slot], masked[:, :], SLOPE, masked[:, :],
                                             op0=ALU.mult, op1=ALU.min).then_inc(leaky_ready, 1)

                def mask_scores(it, k):
                    col = k % K
                    if k == K:
                        eng.wait_ge(least_ready, it + 2)
                    eng.wait_ge(leaky_ready, it * K + k)
                    eng.wait_ge(mask_ready, it * K + k + 1)
                    eng.wait_ge(scores_ready, it * K + k + 1)
                    stand_alone(eng)
                    eng.tensor_tensor_reduce(masked[:, :], mask[:, k % MASK_SLOTS], scores[:, k % 2], 1.0, 3.0e38, ALU.add,
                                             ALU.min, neg_max[:, col:col + 1]).then_inc(masked_ready, 1)
                    eng.wait_ge(masked_ready, it * K + k + 1)
                    if k >= 2:
                        eng.wait_ge(prob_ready, it * K + k - 1)
                    leaky_relu(it * K + k, k % 2, col)

                def finish(g, k, slot, x_slot, t, stores):
                    eng.wait_ge(prob_ready, g + 1)
                    eng.reciprocal(inv_sum[:, k:k + 1], row_sum[:, k:k + 1]).then_inc(inv_ready, 1)
                    eng.wait_ge(inv_ready, g + 1)
                    eng.wait_ge(agg_ready, g + 2)
                    if k % STORE == 0:
                        eng.wait_ge(stored[slot], stores * 16 + 1)
                    eng.scalar_tensor_tensor(o_sb[:, slot, k % STORE], agg[:, :], inv_sum[:, k:k + 1],
                                             x_sb[:, x_slot, t], op0=ALU.mult, op1=ALU.add).then_inc(o_ready, 1)

                def body(it, last):
                    for k in range(K):
                        if not (last and k + 2 >= K):
                            mask_scores(it, k + 2)
                        if k % T in STATS_STEPS and not (last and k > T):
                            slot = (k // T + 1) % 2
                            eng.wait_ge(x_loaded[slot], (it + k // T + 1) * 16)
                            n = T // len(STATS_STEPS)
                            i = STATS_STEPS.index(k % T)
                            moments(it * BPI + k // T + 1, slot, range(i * n, (i + 1) * n))
                        finish(it * K + k, k, k // STORE, k // T, k % T, it)
                        if k % T in TURN_STEPS and not (last and k > T):
                            scale_hT(it * BPI + k // T + 1, (k // T + 1) % 2, TURN_STEPS.index(k % T), [((k // T + 1) % 2, 0)])
                        if k == K - 3:
                            eng.wait_ge(least_ready, it + 1)
                            eng.tensor_tensor(least[:, :], least[:, :], neg_max[:, :], ALU.min).then_inc(least_ready, 1)

                eng.sem_inc(o_ready, 1)
                eng.sem_inc(compared, 1)
                eng.memset(least[:, :], 3.0e38).then_inc(least_ready, 1)
                eng.wait_ge(a_loaded, 64)
                eng.tensor_scalar(neg_a[:, :], a_col[:, :], -1.0, None, ALU.mult).then_inc(neg_a_ready, 1)
                eng.wait_ge(x_loaded[0], 16)
                moments(0, 0, range(T))
                eng.wait_ge(neg_a_ready, 1)
                for half in range(2):
                    scale_hT(0, 0, half, [(0, 0)])
                mask_scores(0, 0)
                mask_scores(0, 1)
                with eng.Fori(0, ITERS - 1) as it:
                    body(it, False)
                body(ITERS - 1, True)

                eng.wait_ge(least_ready, ITERS + 1)
                eng.tensor_reduce(lane_least[:, :], least[:, :], AX_X, ALU.min).then_inc(lane_least_ready, 1)
                eng.wait_ge(lanes_turned, 1)
                eng.tensor_reduce(all_least[:, :], turn[0:1, 0:P], AX_X, ALU.min).then_inc(all_least_ready, 1)
                eng.wait_ge(all_least_ready, 1)
                eng.tensor_scalar(flag[:, :], all_least[:, :], FLAG_BELOW, None, ALU.is_lt).then_inc(flag_ready, 1)

                eng.wait_ge(flag_ready, 1)
                with eng.If(eng.value_load(flag[0:1, 0:1]) != 0):
                    with eng.Fori(0, B) as b:
                        eng.wait_ge(x_loaded[0], (b + B // 2 + 1) * 16)
                        moments(b + B, 0, range(T))
                        for half in range(2):
                            scale_hT(b + B, 0, half, [(a, a) for a in range(4)])
                        for t in range(T):
                            slot = t // 2 % ADJ_SLOTS
                            eng.wait_ge(adj_loaded[slot], 16 * (b + 1 + B * T // 2 // ADJ_SLOTS))
                            eng.wait_ge(leaky_ready, (b + B) * T + t)
                            eng.memset(masked[:, :], BIG).then_inc(picked0, 1)
                            for a in range(4):
                                if a:
                                    eng.wait_ge(picked, 4 * (b * T + t) + a)
                                eng.tensor_scalar(hit[:, :], adj_sb[:, slot, t % 2], float(a + 1), None,
                                                  ALU.is_equal).then_inc(hit_ready, 1)
                                eng.wait_ge(hit_ready, 4 * (b * T + t) + a + 1)
                                if a == 0:
                                    eng.wait_ge(picked0, b * T + t + 1)
                                if a == 3:
                                    eng.sem_inc(compared, 1)
                                eng.wait_ge(scores_ready, B * T + 4 * (b * T + t) + a + 1)
                                stand_alone(eng)
                                eng.copy_predicated(masked[:, :], hit[:, :], scores[:, a % 2]).then_inc(picked, 1)
                            eng.wait_ge(picked, 4 * (b * T + t) + 4)
                            eng.tensor_reduce(neg_max[:, t:t + 1], masked[:, :], AX_X, ALU.min).then_inc(least_of_row, 1)
                            eng.wait_ge(least_of_row, b * T + t + 1)
                            leaky_relu(b, 0, t)
                            finish((b + B) * T + t, t, t // STORE, 0, t, b + ITERS)


_INS = ["x", "adj", "L0_gnn_a0", "L0_gnn_a1", "L0_gnn_a2", "L0_gnn_a3"]


def kernel(**inputs):
    import numpy as np
    import concourse.bacc as bacc
    from concourse.bass_utils import run_bass_kernel_spmd

    nc = bacc.Bacc("TRN2", target_bir_lowering=False, num_devices=1)
    arrays, args = {}, []
    for name in _INS:
        a = np.ascontiguousarray(inputs[name])
        arrays[f"in_{name}"] = a
        args.append(nc.dram_tensor(f"in_{name}", a.shape, mybir.dt.from_np(a.dtype), kind="ExternalInput").ap())
    shape = inputs["x"].shape
    args.append(nc.dram_tensor("out", shape, F32, kind="ExternalOutput").ap())
    build(nc, *args)
    r = run_bass_kernel_spmd(nc, [arrays], core_ids=[0])
    return r.results[0]["out"]
```

```python
from contextlib import ExitStack

import concourse.bass as bass
from concourse import mybir

F32 = mybir.dt.float32
F32R = mybir.dt.float32r
BF16 = mybir.dt.bfloat16
I32 = mybir.dt.int32
U32 = mybir.dt.uint32
ALU = mybir.AluOpType
ACT = mybir.ActivationFunctionType
AX_X = mybir.AxisListType.X

P = 128
SLOPE = 0.2
EPS = 1e-5
BIG = 2.0 ** 90
FLAG_BELOW = -(2.0 ** 80)


def build(nc, x, adj, a0, a1, a2, a3, out):
    B, N, D = x.shape
    T = N // P
    BPI = 2
    K = BPI * T
    ITERS = B // BPI
    assert D == P and N == 1024 and B % BPI == 0
    HALF = N // 2
    ADJ_SLOTS = 4
    MASK_SLOTS = 4
    STORE = 4
    OUT_SLOTS = K // STORE
    STATS_STEPS, NORM_STEPS, TURN_STEPS, SPLIT_STEPS = (1, 2), (2, 3), (3, 4), (4, 5)
    HT = T // 2

    ctx = ExitStack()
    with ctx:
        def sb(name, shape, dt=F32):
            return ctx.enter_context(nc.sbuf_tensor(name, shape, dt))

        def ps(name, shape, dt=F32):
            return ctx.enter_context(nc.psum_tensor(name, shape, dt))

        def sem(name):
            return ctx.enter_context(nc.semaphore(name))

        ident = sb("ident", [P, P])
        neg_half = sb("neg_half", [P, T])
        a_col = sb("a_col", [P, 4])
        neg_a = sb("neg_a", [P, 4])
        x_sb = sb("x_sb", [P, 2, T, D])
        h_sb = sb("h_sb", [P, 2, T, D])
        hT_hi = sb("hT_hi", [P, 2, N], F32R)
        hT_lo = sb("hT_lo", [P, 2, N], F32R)
        haT_hi = sb("haT_hi", [P, 4, N], F32R)
        haT_lo = sb("haT_lo", [P, 4, N], F32R)
        stats = sb("stats", [P, T, 6])
        mv = sb("mv", [P, T, 2])
        neg_mean = sb("neg_mean", [P, T])
        var_eps = sb("var_eps", [P, T])
        rstd = sb("rstd", [P, T])
        shift = sb("shift", [P, T])
        adj_sb = sb("adj_sb", [P, ADJ_SLOTS, 2, N], I32)
        mask = sb("mask", [P, MASK_SLOTS, N], BF16)
        masked = sb("masked", [P, N])
        leaky = sb("leaky", [P, 2, N])
        prob = sb("prob", [P, 2, N])
        probT = sb("probT", [P, N])
        neg_max = sb("neg_max", [P, K])
        bias = sb("bias", [P, K])
        row_sum = sb("row_sum", [P, K])
        inv_sum = sb("inv_sum", [P, K])
        least = sb("least", [P, K])
        lane_least = sb("lane_least", [P, 1])
        all_least = sb("all_least", [1, 1])
        hit = sb("hit", [P, N], I32)
        flag = sb("flag", [1, 1], I32)
        o_sb = sb("o_sb", [P, OUT_SLOTS, STORE, D])

        scores = ps("scores", [P, 2, N])
        pT = ps("pT", [P, 2, HALF])
        agg = ps("agg", [P, D])
        turn = ps("turn", [P, HALF])

        a_loaded = sem("a_loaded")
        waits_taken = sem("waits_taken")
        x_loaded = [sem(f"x_loaded{i}") for i in range(2)]
        adj_loaded = [sem(f"adj_loaded{i}") for i in range(ADJ_SLOTS)]
        zeroed = sem("zeroed")
        ident_ready = sem("ident_ready")
        neg_a_ready = sem("neg_a_ready")
        stats_ready = sem("stats_ready")
        mv_ready = sem("mv_ready")
        moments_ready = sem("moments_ready")
        rstd_ready = sem("rstd_ready")
        shift_ready = sem("shift_ready")
        h_ready = sem("h_ready")
        turned = sem("turned")
        hi_ready = sem("hi_ready")
        lo_ready = sem("lo_ready")
        mask_ready = sem("mask_ready")
        scores_ready = sem("scores_ready")
        masked_ready = sem("masked_ready")
        bias_ready = sem("bias_ready")
        leaky_ready = sem("leaky_ready")
        prob_ready = sem("prob_ready")
        pT_ready = sem("pT_ready")
        probT_ready = sem("probT_ready")
        agg_ready = sem("agg_ready")
        inv_ready = sem("inv_ready")
        o_ready = sem("o_ready")
        least_ready = sem("least_ready")
        lane_least_ready = sem("lane_least_ready")
        lanes_turned = sem("lanes_turned")
        all_least_ready = sem("all_least_ready")
        hit_ready = sem("hit_ready")
        picked0 = sem("picked0")
        picked = sem("picked")
        compared = sem("compared")
        least_of_row = sem("least_of_row")
        flag_ready = sem("flag_ready")
        stored = [sem(f"stored{i}") for i in range(OUT_SLOTS)]

        x_v = x.rearrange("b (t p) d -> b p t d", p=P)
        out_v = out.rearrange("b (t p) d -> b p t d", p=P)
        adj_v = adj.rearrange("b (t p) n -> b p t n", p=P)

        def stand_alone(eng):
            eng.sem_inc(waits_taken, 1)

        with nc.Block() as block:

            @block.sync
            def _(eng):
                def load_x(b, slot):
                    eng.dma_start(x_sb[:, slot], x_v[b]).then_inc(x_loaded[slot], 16)

                def load_adj(b, t):
                    slot = t // 2 % ADJ_SLOTS
                    eng.dma_start(adj_sb[:, slot], adj_v[b, :, t:t + 2, :]).then_inc(adj_loaded[slot], 16)

                def store(b, q, slot, done):
                    eng.wait_ge(o_ready, done + 1)
                    eng.dma_start(out_v[b, :, STORE * q:STORE * (q + 1), :],
                                  o_sb[:, slot]).then_inc(stored[slot], 16)

                def store_of(it, q):
                    store(it * BPI + q * STORE // T, q % (T // STORE), q, it * K + (q + 1) * STORE)

                def body(it, last):
                    for k in range(0, K, 2):
                        if k % T == 0 and not (last and k):
                            eng.wait_ge(o_ready, it * K + k + 1)
                            load_x(it * BPI + k // T + 1, (k // T + 1) % 2)
                        ahead = k + 2 * ADJ_SLOTS
                        if not (last and ahead >= K):
                            eng.wait_ge(mask_ready, it * K + k + 2)
                            load_adj(it * BPI + ahead // T, ahead % T)
                        if k and k % STORE == 0:
                            store_of(it, k // STORE - 1)
                    store_of(it, OUT_SLOTS - 1)

                for s in stored:
                    eng.sem_inc(s, 1)
                load_x(0, 0)
                for i, a in enumerate((a0, a1, a2, a3)):
                    eng.dma_start(a_col[:, i:i + 1], a.rearrange("(d o) -> d o", o=1)).then_inc(a_loaded, 16)
                for s in range(ADJ_SLOTS):
                    load_adj(0, 2 * s)
                with eng.Fori(0, ITERS - 1) as it:
                    body(it, False)
                body(ITERS - 1, True)
                for s in stored:
                    eng.wait_ge(s, 16 * ITERS + 1)

                eng.wait_ge(flag_ready, 1)
                with eng.If(eng.value_load(flag[0:1, 0:1]) != 0):
                    with eng.Fori(0, B) as b:
                        eng.wait_ge(o_ready, (b + B) * T + 1)
                        load_x(b, 0)
                        eng.wait_ge(compared, b * T + 1)
                        for s in range(ADJ_SLOTS):
                            load_adj(b, 2 * s)
                        for q in range(T // STORE):
                            store(b, q, q, (b + B) * T + (q + 1) * STORE)
                    for q in range(T // STORE):
                        eng.wait_ge(stored[q], 16 * (ITERS + B) + 1)

            @block.gpsimd
            def _(eng):
                def convert(loads, k):
                    eng.wait_ge(adj_loaded[k // 2 % ADJ_SLOTS], 16 * loads)
                    stand_alone(eng)
                    eng.tensor_scalar(mask[:, k % MASK_SLOTS], adj_sb[:, k // 2 % ADJ_SLOTS, k % 2].bitcast(U32),
                                      -BIG, BIG, ALU.mult, ALU.add).then_inc(mask_ready, 1)

                def norm_factors(c, half):
                    cols = slice(half * HT, (half + 1) * HT)
                    eng.wait_ge(mv_ready, c * T + (half + 1) * HT)
                    stand_alone(eng)
                    eng.tensor_scalar(neg_mean[:, cols], mv[:, cols, 0], -1.0, 0.0, ALU.mult, ALU.add).then_inc(moments_ready, 1)
                    eng.tensor_scalar(var_eps[:, cols], mv[:, cols, 1], EPS, 1.0, ALU.add, ALU.mult).then_inc(moments_ready, 1)
                    eng.wait_ge(moments_ready, 4 * c + 2 * half + 2)
                    eng.tensor_tensor(rstd[:, cols], var_eps[:, cols], neg_half[:, cols], ALU.pow).then_inc(rstd_ready, 1)
                    eng.wait_ge(rstd_ready, 2 * c + half + 1)
                    eng.tensor_tensor(shift[:, cols], neg_mean[:, cols], rstd[:, cols], ALU.mult).then_inc(shift_ready, 1)

                def body(it, last):
                    for k in range(K):
                        ahead = k + MASK_SLOTS
                        if not (last and ahead >= K):
                            eng.wait_ge(masked_ready, it * K + k + 1)
                            convert(it * (K // 2 // ADJ_SLOTS) + ahead // 2 // ADJ_SLOTS + 1, ahead)
                        if k % T in STATS_STEPS and not (last and k > T):
                            norm_factors(it * BPI + k // T + 1, STATS_STEPS.index(k % T))

                eng.memset(ident[:, :], 0.0).then_inc(zeroed, 1)
                eng.memset(neg_half[:, :], -0.5).then_inc(zeroed, 1)
                eng.wait_ge(zeroed, 2)
                eng.affine_select(out=ident[:, :], in_=ident[:, :], compare_op=ALU.not_equal, fill=1.0,
                                  base=0, pattern=[[-1, P]], channel_multiplier=1).then_inc(ident_ready, 1)
                for half in range(2):
                    norm_factors(0, half)
                for k in range(MASK_SLOTS):
                    convert(1, k)
                with eng.Fori(0, ITERS - 1) as it:
                    body(it, False)
                body(ITERS - 1, True)

                eng.wait_ge(flag_ready, 1)
                with eng.If(eng.value_load(flag[0:1, 0:1]) != 0):
                    with eng.Fori(0, B) as b:
                        for half in range(2):
                            norm_factors(b + B, half)

            @block.tensor
            def _(eng):
                def turn_h(c, slot, half):
                    eng.wait_ge(h_ready, c * T + (half + 1) * HT)
                    if not (type(c) is int and c == half == 0):
                        eng.wait_ge(lo_ready, 2 * c + half)
                    for j in range(HT):
                        ins = eng.transpose(turn[:, j * P:(j + 1) * P], h_sb[:, slot, half * HT + j], ident[:, :])
                    ins.then_inc(turned, 1)

                def score(bank, slot, t, which):
                    rows = slice(t * P, (t + 1) * P)
                    for n, (left, right) in enumerate(((haT_lo, hT_hi), (haT_hi, hT_lo), (haT_hi, hT_hi))):
                        for j in range(2):
                            cols = slice(j * HALF, (j + 1) * HALF)
                            ins = eng.matmul(scores[:, bank, cols], left[:, which, rows], right[:, slot, cols],
                                             start=(n == 0), stop=(n == 2))
                    ins.then_inc(scores_ready, 1)

                def score_tile(it, k):
                    if k % T == 0:
                        eng.wait_ge(lo_ready, 2 * (it * BPI + k // T) + 2)
                    if k >= 2:
                        eng.wait_ge(masked_ready, it * K + k - 1)
                    score(k % 2, k // T % 2, k % T, k // T % 2)

                def turn_prob(g, src):
                    eng.wait_ge(prob_ready, g + 1)
                    for j in range(2):
                        for i in range(T // 2):
                            b = j * T // 2 + i
                            ins = eng.transpose(pT[:, j, i * P:(i + 1) * P], prob[:, src, b * P:(b + 1) * P], ident[:, :])
                        ins.then_inc(pT_ready, 1)

                def aggregate(g, slot):
                    eng.wait_ge(o_ready, g + 1)
                    for b in range(T):
                        if b % (T // 2) == 0:
                            eng.wait_ge(probT_ready, g * 2 + 1 + b // (T // 2))
                        ins = eng.matmul(agg[:, :], probT[:, b * P:(b + 1) * P], h_sb[:, slot, b],
                                         start=(b == 0), stop=(b == T - 1))
                    ins.then_inc(agg_ready, 1)

                def body(it, last):
                    for k in range(K):
                        turn_prob(it * K + k, k % 2)
                        if not (last and k + 2 >= K):
                            score_tile(it, k + 2)
                        aggregate(it * K + k, k // T)
                        if k % T in TURN_STEPS and not (last and k > T):
                            turn_h(it * BPI + k // T + 1, (k // T + 1) % 2, TURN_STEPS.index(k % T))

                eng.sem_inc(agg_ready, 1)
                eng.wait_ge(ident_ready, 1)
                for half in range(2):
                    turn_h(0, 0, half)
                score_tile(0, 0)
                score_tile(0, 1)
                with eng.Fori(0, ITERS - 1) as it:
                    body(it, False)
                body(ITERS - 1, True)

                eng.wait_ge(lane_least_ready, 1)
                eng.transpose(turn[0:1, 0:P], lane_least[:, :], ident[:, :]).then_inc(lanes_turned, 1)

                eng.wait_ge(flag_ready, 1)
                with eng.If(eng.value_load(flag[0:1, 0:1]) != 0):
                    with eng.Fori(0, B) as b:
                        for half in range(2):
                            turn_h(b + B, 0, half)
                        eng.wait_ge(lo_ready, 2 * (b + B) + 2)
                        for t in range(T):
                            for a in range(4):
                                if a >= 2:
                                    eng.wait_ge(picked, 4 * (b * T + t) + a - 1)
                                score(a % 2, 0, t, a)
                            turn_prob((b + B) * T + t, 0)
                            aggregate((b + B) * T + t, 0)

            @block.scalar
            def _(eng):
                def copy_probT(g):
                    for j in range(2):
                        eng.wait_ge(pT_ready, g * 2 + j + 1)
                        nc.scalar.copy(probT[:, j * HALF:(j + 1) * HALF], pT[:, j]).then_inc(probT_ready, 1)

                def exponential(g, slot, col):
                    eng.wait_ge(leaky_ready, g + 1)
                    nc.scalar.activation(prob[:, slot], leaky[:, slot], ACT.Exp, bias=bias[:, col:col + 1], scale=-1.0,
                                         accum_out=row_sum[:, col:col + 1]).then_inc(prob_ready, 1)

                def normalise(c, slot, half):
                    eng.wait_ge(shift_ready, 2 * c + half + 1)
                    for t in range(half * HT, (half + 1) * HT):
                        nc.scalar.activation(h_sb[:, slot, t], x_sb[:, slot, t], ACT.Relu, bias=shift[:, t:t + 1],
                                             scale=rstd[:, t:t + 1]).then_inc(h_ready, 1)

                def round_hT(c, slot, half, slots):
                    cols = slice(half * HALF, (half + 1) * HALF)
                    eng.wait_ge(turned, c * 2 + half + 1)
                    nc.scalar.copy(hT_hi[:, slot, cols], turn[:, :])
                    for to, a in slots:
                        ins = nc.scalar.activation(haT_hi[:, to, cols], turn[:, :], ACT.Copy, scale=neg_a[:, a:a + 1])
                    ins.then_inc(hi_ready, 1)

                def body(it, last):
                    for k in range(K):
                        copy_probT(it * K + k)
                        if not (last and k + 1 >= K):
                            exponential(it * K + k + 1, (k + 1) % 2, (k + 1) % K)
                        c, slot = it * BPI + k // T + 1, (k // T + 1) % 2
                        if k % T in NORM_STEPS and not (last and k > T):
                            if k % T == NORM_STEPS[0]:
                                eng.wait_ge(agg_ready, (c - 1) * T + 1)
                            normalise(c, slot, NORM_STEPS.index(k % T))
                        if k % T in TURN_STEPS and not (last and k > T):
                            round_hT(c, slot, TURN_STEPS.index(k % T), [(slot, 0)])

                eng.wait_ge(neg_a_ready, 1)
                for half in range(2):
                    normalise(0, 0, half)
                for half in range(2):
                    round_hT(0, 0, half, [(0, 0)])
                exponential(0, 0, 0)
                with eng.Fori(0, ITERS - 1) as it:
                    body(it, False)
                body(ITERS - 1, True)

                eng.wait_ge(flag_ready, 1)
                with eng.If(eng.value_load(flag[0:1, 0:1]) != 0):
                    with eng.Fori(0, B) as b:
                        eng.wait_ge(agg_ready, (b + B) * T + 1)
                        for half in range(2):
                            normalise(b + B, 0, half)
                        for half in range(2):
                            round_hT(b + B, 0, half, [(a, a) for a in range(4)])
                        for t in range(T):
                            exponential((b + B) * T + t, 0, t)
                            copy_probT((b + B) * T + t)

            @block.vector
            def _(eng):
                def moments(c, slot, tiles):
                    for t in tiles:
                        eng.bn_stats(stats[:, t], x_sb[:, slot, t]).then_inc(stats_ready, 1)
                    eng.wait_ge(stats_ready, c * T + tiles[-1] + 1)
                    stand_alone(eng)
                    for t in tiles:
                        eng.bn_aggr(mv[:, t], stats[:, t]).then_inc(mv_ready, 1)

                def split_hT(c, slot, half, slots):
                    cols = slice(half * HALF, (half + 1) * HALF)
                    eng.wait_ge(hi_ready, c * 2 + half + 1)
                    eng.tensor_tensor(hT_lo[:, slot, cols], turn[:, :], hT_hi[:, slot, cols].bitcast(F32), ALU.subtract)
                    for to, a in slots:
                        ins = eng.scalar_tensor_tensor(haT_lo[:, to, cols], turn[:, :], neg_a[:, a:a + 1],
                                                       haT_hi[:, to, cols].bitcast(F32), op0=ALU.mult, op1=ALU.subtract)
                    ins.then_inc(lo_ready, 1)

                def leaky_relu(g, slot, col):
                    eng.scalar_tensor_tensor(bias[:, col:col + 1], neg_max[:, col:col + 1], SLOPE, neg_max[:, col:col + 1],
                                             op0=ALU.mult, op1=ALU.min).then_inc(bias_ready, 1)
                    eng.scalar_tensor_tensor(leaky[:, slot], masked[:, :], SLOPE, masked[:, :],
                                             op0=ALU.mult, op1=ALU.min).then_inc(leaky_ready, 1)

                def mask_scores(it, k):
                    col = k % K
                    if k == K:
                        eng.wait_ge(least_ready, it + 2)
                    eng.wait_ge(leaky_ready, it * K + k)
                    eng.wait_ge(mask_ready, it * K + k + 1)
                    eng.wait_ge(scores_ready, it * K + k + 1)
                    stand_alone(eng)
                    eng.tensor_tensor_reduce(masked[:, :], mask[:, k % MASK_SLOTS], scores[:, k % 2], 1.0, 3.0e38, ALU.add,
                                             ALU.min, neg_max[:, col:col + 1]).then_inc(masked_ready, 1)
                    eng.wait_ge(masked_ready, it * K + k + 1)
                    if k >= 2:
                        eng.wait_ge(prob_ready, it * K + k - 1)
                    leaky_relu(it * K + k, k % 2, col)

                def finish(g, k, slot, x_slot, t, stores):
                    eng.wait_ge(prob_ready, g + 1)
                    eng.reciprocal(inv_sum[:, k:k + 1], row_sum[:, k:k + 1]).then_inc(inv_ready, 1)
                    eng.wait_ge(inv_ready, g + 1)
                    eng.wait_ge(agg_ready, g + 2)
                    if k % STORE == 0:
                        eng.wait_ge(stored[slot], stores * 16 + 1)
                    eng.scalar_tensor_tensor(o_sb[:, slot, k % STORE], agg[:, :], inv_sum[:, k:k + 1],
                                             x_sb[:, x_slot, t], op0=ALU.mult, op1=ALU.add).then_inc(o_ready, 1)

                def body(it, last):
                    for k in range(K):
                        if k % T in SPLIT_STEPS and not (last and k > T):
                            slot = (k // T + 1) % 2
                            split_hT(it * BPI + k // T + 1, slot, SPLIT_STEPS.index(k % T), [(slot, 0)])
                        if not (last and k + 2 >= K):
                            mask_scores(it, k + 2)
                        if k % T in STATS_STEPS and not (last and k > T):
                            slot = (k // T + 1) % 2
                            eng.wait_ge(x_loaded[slot], (it + k // T + 1) * 16)
                            i = STATS_STEPS.index(k % T)
                            moments(it * BPI + k // T + 1, slot, range(i * HT, (i + 1) * HT))
                        finish(it * K + k, k, k // STORE, k // T, k % T, it)
                        if k == K - 3:
                            eng.wait_ge(least_ready, it + 1)
                            eng.tensor_tensor(least[:, :], least[:, :], neg_max[:, :], ALU.min).then_inc(least_ready, 1)

                eng.sem_inc(o_ready, 1)
                eng.sem_inc(compared, 1)
                eng.memset(least[:, :], 3.0e38).then_inc(least_ready, 1)
                eng.wait_ge(a_loaded, 64)
                eng.tensor_scalar(neg_a[:, :], a_col[:, :], -1.0, None, ALU.mult).then_inc(neg_a_ready, 1)
                eng.wait_ge(x_loaded[0], 16)
                for half in range(2):
                    moments(0, 0, range(half * HT, (half + 1) * HT))
                for half in range(2):
                    split_hT(0, 0, half, [(0, 0)])
                mask_scores(0, 0)
                mask_scores(0, 1)
                with eng.Fori(0, ITERS - 1) as it:
                    body(it, False)
                body(ITERS - 1, True)

                eng.wait_ge(least_ready, ITERS + 1)
                eng.tensor_reduce(lane_least[:, :], least[:, :], AX_X, ALU.min).then_inc(lane_least_ready, 1)
                eng.wait_ge(lanes_turned, 1)
                eng.tensor_reduce(all_least[:, :], turn[0:1, 0:P], AX_X, ALU.min).then_inc(all_least_ready, 1)
                eng.wait_ge(all_least_ready, 1)
                eng.tensor_scalar(flag[:, :], all_least[:, :], FLAG_BELOW, None, ALU.is_lt).then_inc(flag_ready, 1)

                eng.wait_ge(flag_ready, 1)
                with eng.If(eng.value_load(flag[0:1, 0:1]) != 0):
                    with eng.Fori(0, B) as b:
                        eng.wait_ge(x_loaded[0], (b + B // 2 + 1) * 16)
                        moments(b + B, 0, range(T))
                        for half in range(2):
                            split_hT(b + B, 0, half, [(a, a) for a in range(4)])
                        for t in range(T):
                            slot = t // 2 % ADJ_SLOTS
                            eng.wait_ge(adj_loaded[slot], 16 * (b + 1 + B * T // 2 // ADJ_SLOTS))
                            eng.wait_ge(leaky_ready, (b + B) * T + t)
                            eng.memset(masked[:, :], BIG).then_inc(picked0, 1)
                            for a in range(4):
                                if a:
                                    eng.wait_ge(picked, 4 * (b * T + t) + a)
                                eng.tensor_scalar(hit[:, :], adj_sb[:, slot, t % 2], float(a + 1), None,
                                                  ALU.is_equal).then_inc(hit_ready, 1)
                                eng.wait_ge(hit_ready, 4 * (b * T + t) + a + 1)
                                if a == 0:
                                    eng.wait_ge(picked0, b * T + t + 1)
                                if a == 3:
                                    eng.sem_inc(compared, 1)
                                eng.wait_ge(scores_ready, B * T + 4 * (b * T + t) + a + 1)
                                stand_alone(eng)
                                eng.copy_predicated(masked[:, :], hit[:, :], scores[:, a % 2]).then_inc(picked, 1)
                            eng.wait_ge(picked, 4 * (b * T + t) + 4)
                            eng.tensor_reduce(neg_max[:, t:t + 1], masked[:, :], AX_X, ALU.min).then_inc(least_of_row, 1)
                            eng.wait_ge(least_of_row, b * T + t + 1)
                            leaky_relu(b, 0, t)
                            finish((b + B) * T + t, t, t // STORE, 0, t, b + ITERS)


_INS = ["x", "adj", "L0_gnn_a0", "L0_gnn_a1", "L0_gnn_a2", "L0_gnn_a3"]


def kernel(**inputs):
    import numpy as np
    import concourse.bacc as bacc
    from concourse.bass_utils import run_bass_kernel_spmd

    nc = bacc.Bacc("TRN2", target_bir_lowering=False, num_devices=1)
    arrays, args = {}, []
    for name in _INS:
        a = np.ascontiguousarray(inputs[name])
        arrays[f"in_{name}"] = a
        args.append(nc.dram_tensor(f"in_{name}", a.shape, mybir.dt.from_np(a.dtype), kind="ExternalInput").ap())
    shape = inputs["x"].shape
    args.append(nc.dram_tensor("out", shape, F32, kind="ExternalOutput").ap())
    build(nc, *args)
    r = run_bass_kernel_spmd(nc, [arrays], core_ids=[0])
    return r.results[0]["out"]
```

```python
from contextlib import ExitStack

import concourse.bass as bass
from concourse import mybir

F32 = mybir.dt.float32
F32R = mybir.dt.float32r
BF16 = mybir.dt.bfloat16
I32 = mybir.dt.int32
U32 = mybir.dt.uint32
ALU = mybir.AluOpType
ACT = mybir.ActivationFunctionType
AX_X = mybir.AxisListType.X

P = 128
SLOPE = 0.2
EPS = 1e-5
BIG = 2.0 ** 90
FLAG_BELOW = -(2.0 ** 80)


def build(nc, x, adj, a0, a1, a2, a3, out):
    B, N, D = x.shape
    T = N // P
    BPI = 2
    K = BPI * T
    ITERS = B // BPI
    assert D == P and N == 1024 and B % BPI == 0
    HALF = N // 2
    ADJ_SLOTS = 4
    MASK_SLOTS = 4
    STORE = 4
    OUT_SLOTS = K // STORE
    STATS_STEPS = (6, 7)
    MOMENTS_STEPS, NORM_STEPS, TURN_STEPS, SPLIT_STEPS = (0, 1), (2, 3), (3, 4), (4, 5)
    WARM_UP = 16
    HT = T // 2

    ctx = ExitStack()
    with ctx:
        def sb(name, shape, dt=F32):
            return ctx.enter_context(nc.sbuf_tensor(name, shape, dt))

        def ps(name, shape, dt=F32):
            return ctx.enter_context(nc.psum_tensor(name, shape, dt))

        def sem(name):
            return ctx.enter_context(nc.semaphore(name))

        ident = sb("ident", [P, P])
        neg_half = sb("neg_half", [P, T])
        a_col = sb("a_col", [P, 4])
        neg_a = sb("neg_a", [P, 4])
        x_in = sb("x_in", [P, T, D])
        x_kept = sb("x_kept", [P, 2, T, D])
        h_sb = sb("h_sb", [P, 2, T, D])
        hT_hi = sb("hT_hi", [P, 2, N], F32R)
        hT_lo = sb("hT_lo", [P, 2, N], F32R)
        haT_hi = sb("haT_hi", [P, 4, N], F32R)
        haT_lo = sb("haT_lo", [P, 4, N], F32R)
        stats = sb("stats", [P, T, 6])
        mv = sb("mv", [P, T, 2])
        neg_mean = sb("neg_mean", [P, T])
        var_eps = sb("var_eps", [P, T])
        rstd = sb("rstd", [P, T])
        shift = sb("shift", [P, T])
        adj_sb = sb("adj_sb", [P, ADJ_SLOTS, 2, N], I32)
        mask = sb("mask", [P, MASK_SLOTS, N], BF16)
        masked = sb("masked", [P, N])
        leaky = sb("leaky", [P, 2, N])
        prob = sb("prob", [P, 2, N])
        probT = sb("probT", [P, N])
        neg_max = sb("neg_max", [P, K])
        bias = sb("bias", [P, K])
        row_sum = sb("row_sum", [P, K])
        inv_sum = sb("inv_sum", [P, K])
        least = sb("least", [P, K])
        lane_least = sb("lane_least", [P, 1])
        all_least = sb("all_least", [1, 1])
        hit = sb("hit", [P, N], I32)
        flag = sb("flag", [1, 1], I32)
        o_sb = sb("o_sb", [P, OUT_SLOTS, STORE, D])

        scores = ps("scores", [P, 2, N])
        pT = ps("pT", [P, 2, HALF])
        agg = ps("agg", [P, D])
        turn = ps("turn", [P, HALF])

        FIRST_TURN = (turn[:, :], pT[:, 0])

        a_loaded = sem("a_loaded")
        waits_taken = sem("waits_taken")
        x_loaded = sem("x_loaded")
        first_x_loaded = sem("first_x_loaded")
        x_copied = sem("x_copied")
        adj_loaded = [sem(f"adj_loaded{i}") for i in range(ADJ_SLOTS)]
        zeroed = sem("zeroed")
        ident_ready = sem("ident_ready")
        neg_a_ready = sem("neg_a_ready")
        stats_ready = sem("stats_ready")
        mv_ready = sem("mv_ready")
        moments_ready = sem("moments_ready")
        rstd_ready = sem("rstd_ready")
        shift_ready = sem("shift_ready")
        first_scaled = sem("first_scaled")
        second_half_ready = sem("second_half_ready")
        h_ready = sem("h_ready")
        turned = sem("turned")
        hi_ready = sem("hi_ready")
        lo_ready = sem("lo_ready")
        mask_ready = sem("mask_ready")
        scores_ready = sem("scores_ready")
        masked_ready = sem("masked_ready")
        bias_ready = sem("bias_ready")
        leaky_ready = sem("leaky_ready")
        prob_ready = sem("prob_ready")
        pT_ready = sem("pT_ready")
        probT_ready = sem("probT_ready")
        agg_ready = sem("agg_ready")
        inv_ready = sem("inv_ready")
        o_ready = sem("o_ready")
        least_ready = sem("least_ready")
        lane_least_ready = sem("lane_least_ready")
        lanes_turned = sem("lanes_turned")
        all_least_ready = sem("all_least_ready")
        hit_ready = sem("hit_ready")
        picked0 = sem("picked0")
        picked = sem("picked")
        compared = sem("compared")
        least_of_row = sem("least_of_row")
        flag_ready = sem("flag_ready")
        stored = [sem(f"stored{i}") for i in range(OUT_SLOTS)]

        x_v = x.rearrange("b (t p) d -> b p t d", p=P)
        out_v = out.rearrange("b (t p) d -> b p t d", p=P)
        adj_v = adj.rearrange("b (t p) n -> b p t n", p=P)

        def stand_alone(eng):
            eng.sem_inc(waits_taken, 1)

        with nc.Block() as block:

            @block.sync
            def _(eng):
                def load_x(c, b):
                    eng.wait_ge(h_ready, c * T)
                    eng.wait_ge(x_copied, c)
                    eng.dma_start(x_in[:, :, :], x_v[b]).then_inc(x_loaded, 16)

                def load_adj(b, t):
                    slot = t // 2 % ADJ_SLOTS
                    eng.dma_start(adj_sb[:, slot], adj_v[b, :, t:t + 2, :]).then_inc(adj_loaded[slot], 16)

                def store(b, q, slot, done):
                    eng.wait_ge(o_ready, done + 1)
                    eng.dma_start(out_v[b, :, STORE * q:STORE * (q + 1), :],
                                  o_sb[:, slot]).then_inc(stored[slot], 16)

                def store_of(it, q):
                    store(it * BPI + q * STORE // T, q % (T // STORE), q, it * K + (q + 1) * STORE)

                def body(it, last):
                    for k in range(0, K, 2):
                        if k % T == T // 2 and not last:
                            load_x(it * BPI + k // T + 2, it * BPI + k // T + 2)
                        ahead = k + 2 * ADJ_SLOTS
                        if not (last and ahead >= K):
                            eng.wait_ge(mask_ready, it * K + k + 2)
                            load_adj(it * BPI + ahead // T, ahead % T)
                        if k and k % STORE == 0:
                            store_of(it, k // STORE - 1)
                    store_of(it, OUT_SLOTS - 1)

                for s in stored:
                    eng.sem_inc(s, 1)
                eng.dma_start(x_in[:, 0:HT], x_v[0, :, 0:HT]).then_inc(first_x_loaded, 16)
                eng.dma_start(x_in[:, HT:T], x_v[0, :, HT:T]).then_inc(x_loaded, 16)
                for i, a in enumerate((a0, a1, a2, a3)):
                    eng.dma_start(a_col[:, i:i + 1], a.rearrange("(d o) -> d o", o=1)).then_inc(a_loaded, 16)
                for s in range(ADJ_SLOTS):
                    load_adj(0, 2 * s)
                load_x(1, 1)
                with eng.Fori(0, ITERS - 1) as it:
                    body(it, False)
                body(ITERS - 1, True)
                for s in stored:
                    eng.wait_ge(s, 16 * ITERS + 1)

                eng.wait_ge(flag_ready, 1)
                with eng.If(eng.value_load(flag[0:1, 0:1]) != 0):
                    with eng.Fori(0, B) as b:
                        load_x(b + B, b)
                        eng.wait_ge(compared, b * T + 1)
                        for s in range(ADJ_SLOTS):
                            load_adj(b, 2 * s)
                        for q in range(T // STORE):
                            store(b, q, q, (b + B) * T + (q + 1) * STORE)
                    for q in range(T // STORE):
                        eng.wait_ge(stored[q], 16 * (ITERS + B) + 1)

            @block.gpsimd
            def _(eng):
                def convert(loads, k):
                    eng.wait_ge(adj_loaded[k // 2 % ADJ_SLOTS], 16 * loads)
                    stand_alone(eng)
                    eng.tensor_scalar(mask[:, k % MASK_SLOTS], adj_sb[:, k // 2 % ADJ_SLOTS, k % 2].bitcast(U32),
                                      -BIG, BIG, ALU.mult, ALU.add).then_inc(mask_ready, 1)

                def copy_x(c, slot):
                    eng.wait_ge(x_loaded, 16 * (c + 1))
                    if not (type(c) is int and c == 0):
                        eng.wait_ge(o_ready, (c - 1) * T + 1)
                    stand_alone(eng)
                    eng.tensor_scalar(x_kept[:, slot], x_in[:, :, :], 1.0, 0.0, ALU.mult, ALU.add).then_inc(x_copied, 1)

                def norm_factors(c, half):
                    cols = slice(half * HT, (half + 1) * HT)
                    eng.wait_ge(mv_ready, c * T + (half + 1) * HT)
                    stand_alone(eng)
                    eng.tensor_scalar(neg_mean[:, cols], mv[:, cols, 0], -1.0, 0.0, ALU.mult, ALU.add).then_inc(moments_ready, 1)
                    eng.tensor_scalar(var_eps[:, cols], mv[:, cols, 1], EPS, 1.0, ALU.add, ALU.mult).then_inc(moments_ready, 1)
                    eng.wait_ge(moments_ready, 4 * c + 2 * half + 2)
                    eng.tensor_tensor(rstd[:, cols], var_eps[:, cols], neg_half[:, cols], ALU.pow).then_inc(rstd_ready, 1)
                    eng.wait_ge(rstd_ready, 2 * c + half + 1)
                    eng.tensor_tensor(shift[:, cols], neg_mean[:, cols], rstd[:, cols], ALU.mult).then_inc(shift_ready, 1)

                def body(it, last):
                    for k in range(K):
                        ahead = k + MASK_SLOTS
                        if not (last and ahead >= K):
                            eng.wait_ge(masked_ready, it * K + k + 1)
                            convert(it * (K // 2 // ADJ_SLOTS) + ahead // 2 // ADJ_SLOTS + 1, ahead)
                        if k % T in MOMENTS_STEPS and not (last and k >= T):
                            if k % T == MOMENTS_STEPS[0]:
                                copy_x(it * BPI + k // T + 1, (k // T + 1) % 2)
                            norm_factors(it * BPI + k // T + 1, MOMENTS_STEPS.index(k % T))

                eng.memset(ident[:, :], 0.0).then_inc(zeroed, 1)
                eng.memset(neg_half[:, :], -0.5).then_inc(zeroed, 1)
                eng.wait_ge(zeroed, 2)
                eng.affine_select(out=ident[:, :], in_=ident[:, :], compare_op=ALU.not_equal, fill=1.0,
                                  base=0, pattern=[[-1, P]], channel_multiplier=1).then_inc(ident_ready, 1)
                for half in range(2):
                    norm_factors(0, half)
                for k in range(MASK_SLOTS):
                    convert(1, k)
                copy_x(0, 0)
                with eng.Fori(0, ITERS - 1) as it:
                    body(it, False)
                body(ITERS - 1, True)

                eng.wait_ge(flag_ready, 1)
                with eng.If(eng.value_load(flag[0:1, 0:1]) != 0):
                    with eng.Fori(0, B) as b:
                        for half in range(2):
                            norm_factors(b + B, half)
                        eng.wait_ge(o_ready, (b + B) * T + 1)
                        copy_x(b + B, 0)

            @block.tensor
            def _(eng):
                def turn_h(c, slot, half, bank=turn):
                    if type(c) is int and c == 0 and half:
                        eng.wait_ge(second_half_ready, 1)
                    else:
                        eng.wait_ge(h_ready, c * T + (half + 1) * HT)
                    if not (type(c) is int and c == 0):
                        eng.wait_ge(lo_ready, 2 * c + half)
                    for j in range(HT):
                        ins = eng.transpose(bank[:, j * P:(j + 1) * P], h_sb[:, slot, half * HT + j], ident[:, :])
                    ins.then_inc(turned, 1)

                def score(c, bank, slot, t, which):
                    rows = slice(t * P, (t + 1) * P)
                    for j in range(2):
                        if t == 0:
                            eng.wait_ge(lo_ready, 2 * c + j + 1)
                        cols = slice(j * HALF, (j + 1) * HALF)
                        for n, (left, right) in enumerate(((haT_lo, hT_hi), (haT_hi, hT_lo), (haT_hi, hT_hi))):
                            ins = eng.matmul(scores[:, bank, cols], left[:, which, rows], right[:, slot, cols],
                                             start=(n == 0), stop=(n == 2))
                    ins.then_inc(scores_ready, 1)

                def score_tile(it, k):
                    if k >= 2:
                        eng.wait_ge(masked_ready, it * K + k - 1)
                    score(it * BPI + k // T, k % 2, k // T % 2, k % T, k // T % 2)

                def turn_prob(g, src):
                    eng.wait_ge(prob_ready, g + 1)
                    for j in range(2):
                        for i in range(T // 2):
                            b = j * T // 2 + i
                            ins = eng.transpose(pT[:, j, i * P:(i + 1) * P], prob[:, src, b * P:(b + 1) * P], ident[:, :])
                        ins.then_inc(pT_ready, 1)

                def aggregate(g, slot):
                    eng.wait_ge(o_ready, g + 1)
                    for b in range(T):
                        if b % (T // 2) == 0:
                            eng.wait_ge(probT_ready, g * 2 + 1 + b // (T // 2))
                        ins = eng.matmul(agg[:, :], probT[:, b * P:(b + 1) * P], h_sb[:, slot, b],
                                         start=(b == 0), stop=(b == T - 1))
                    ins.then_inc(agg_ready, 1)

                def body(it, last):
                    for k in range(K):
                        if last and k == K - 1:
                            eng.wait_ge(lane_least_ready, 1)
                            eng.transpose(turn[0:1, 0:P], lane_least[:, :], ident[:, :]).then_inc(lanes_turned, 1)
                        turn_prob(it * K + k, k % 2)
                        if not (last and k + 2 >= K):
                            score_tile(it, k + 2)
                        aggregate(it * K + k, k // T)
                        if k % T in TURN_STEPS and not (last and k >= T):
                            turn_h(it * BPI + k // T + 1, (k // T + 1) % 2, TURN_STEPS.index(k % T))

                eng.sem_inc(agg_ready, 1)
                eng.wait_ge(ident_ready, 1)
                for _ in range(WARM_UP):
                    eng.matmul(pT[:, 1, 0:P], ident[:, :], ident[:, :], start=True, stop=True)
                for half in range(2):
                    turn_h(0, 0, half, FIRST_TURN[half])
                score_tile(0, 0)
                score_tile(0, 1)
                with eng.Fori(0, ITERS - 1) as it:
                    body(it, False)
                body(ITERS - 1, True)

                eng.wait_ge(flag_ready, 1)
                with eng.If(eng.value_load(flag[0:1, 0:1]) != 0):
                    with eng.Fori(0, B) as b:
                        for half in range(2):
                            turn_h(b + B, 0, half)
                        for t in range(T):
                            for a in range(4):
                                if a >= 2:
                                    eng.wait_ge(picked, 4 * (b * T + t) + a - 1)
                                score(b + B, a % 2, 0, t, a)
                            turn_prob((b + B) * T + t, 0)
                            aggregate((b + B) * T + t, 0)

            @block.scalar
            def _(eng):
                def copy_probT(g):
                    for j in range(2):
                        eng.wait_ge(pT_ready, g * 2 + j + 1)
                        nc.scalar.copy(probT[:, j * HALF:(j + 1) * HALF], pT[:, j]).then_inc(probT_ready, 1)

                def exponential(g, slot, col):
                    eng.wait_ge(leaky_ready, g + 1)
                    nc.scalar.activation(prob[:, slot], leaky[:, slot], ACT.Exp, bias=bias[:, col:col + 1], scale=-1.0,
                                         accum_out=row_sum[:, col:col + 1]).then_inc(prob_ready, 1)

                def normalise(c, slot, half):
                    eng.wait_ge(shift_ready, 2 * c + half + 1)
                    for t in range(half * HT, (half + 1) * HT):
                        nc.scalar.activation(h_sb[:, slot, t], x_in[:, t], ACT.Relu, bias=shift[:, t:t + 1],
                                             scale=rstd[:, t:t + 1]).then_inc(h_ready, 1)

                def round_hT(c, slot, half, slots, bank=turn):
                    cols = slice(half * HALF, (half + 1) * HALF)
                    eng.wait_ge(turned, c * 2 + half + 1)
                    nc.scalar.copy(hT_hi[:, slot, cols], bank[:, :])
                    for to, a in slots:
                        ins = nc.scalar.activation(haT_hi[:, to, cols], bank[:, :], ACT.Copy, scale=neg_a[:, a:a + 1])
                    ins.then_inc(hi_ready, 1)

                def body(it, last):
                    for k in range(K):
                        copy_probT(it * K + k)
                        if not (last and k + 1 >= K):
                            exponential(it * K + k + 1, (k + 1) % 2, (k + 1) % K)
                        c, slot = it * BPI + k // T + 1, (k // T + 1) % 2
                        if k % T in NORM_STEPS and not (last and k >= T):
                            if k % T == NORM_STEPS[0]:
                                eng.wait_ge(agg_ready, (c - 1) * T + 1)
                            normalise(c, slot, NORM_STEPS.index(k % T))
                        if k % T in TURN_STEPS and not (last and k >= T):
                            round_hT(c, slot, TURN_STEPS.index(k % T), [(slot, 0)])

                eng.preload_act_table(ACT.Exp)
                normalise(0, 0, 0)
                eng.wait_ge(neg_a_ready, 1)
                for half in range(2):
                    round_hT(0, 0, half, [(0, 0)], FIRST_TURN[half])
                eng.sem_inc(h_ready, HT)
                exponential(0, 0, 0)
                with eng.Fori(0, ITERS - 1) as it:
                    body(it, False)
                body(ITERS - 1, True)

                eng.wait_ge(flag_ready, 1)
                with eng.If(eng.value_load(flag[0:1, 0:1]) != 0):
                    with eng.Fori(0, B) as b:
                        eng.wait_ge(agg_ready, (b + B) * T + 1)
                        for half in range(2):
                            normalise(b + B, 0, half)
                        for half in range(2):
                            round_hT(b + B, 0, half, [(a, a) for a in range(4)])
                        for t in range(T):
                            exponential((b + B) * T + t, 0, t)
                            copy_probT((b + B) * T + t)

            @block.vector
            def _(eng):
                def statistics(half):
                    for t in range(half * HT, (half + 1) * HT):
                        eng.bn_stats(stats[:, t], x_in[:, t]).then_inc(stats_ready, 1)

                def moments(c, half):
                    eng.wait_ge(stats_ready, c * T + (half + 1) * HT)
                    stand_alone(eng)
                    for t in range(half * HT, (half + 1) * HT):
                        eng.bn_aggr(mv[:, t], stats[:, t]).then_inc(mv_ready, 1)

                def split_hT(c, slot, half, slots, bank=turn):
                    cols = slice(half * HALF, (half + 1) * HALF)
                    eng.wait_ge(hi_ready, c * 2 + half + 1)
                    eng.tensor_tensor(hT_lo[:, slot, cols], bank[:, :], hT_hi[:, slot, cols].bitcast(F32), ALU.subtract)
                    for to, a in slots:
                        ins = eng.scalar_tensor_tensor(haT_lo[:, to, cols], bank[:, :], neg_a[:, a:a + 1],
                                                       haT_hi[:, to, cols].bitcast(F32), op0=ALU.mult, op1=ALU.subtract)
                    ins.then_inc(lo_ready, 1)

                def leaky_relu(g, slot, col):
                    eng.scalar_tensor_tensor(bias[:, col:col + 1], neg_max[:, col:col + 1], SLOPE, neg_max[:, col:col + 1],
                                             op0=ALU.mult, op1=ALU.min).then_inc(bias_ready, 1)
                    eng.scalar_tensor_tensor(leaky[:, slot], masked[:, :], SLOPE, masked[:, :],
                                             op0=ALU.mult, op1=ALU.min).then_inc(leaky_ready, 1)

                def mask_scores(it, k):
                    col = k % K
                    if k == K:
                        eng.wait_ge(least_ready, it + 2)
                    eng.wait_ge(leaky_ready, it * K + k)
                    eng.wait_ge(mask_ready, it * K + k + 1)
                    eng.wait_ge(scores_ready, it * K + k + 1)
                    stand_alone(eng)
                    eng.tensor_tensor_reduce(masked[:, :], mask[:, k % MASK_SLOTS], scores[:, k % 2], 1.0, 3.0e38, ALU.add,
                                             ALU.min, neg_max[:, col:col + 1]).then_inc(masked_ready, 1)
                    eng.wait_ge(masked_ready, it * K + k + 1)
                    if k >= 2:
                        eng.wait_ge(prob_ready, it * K + k - 1)
                    leaky_relu(it * K + k, k % 2, col)

                def finish(g, k, slot, x_slot, t, stores):
                    eng.wait_ge(prob_ready, g + 1)
                    eng.reciprocal(inv_sum[:, k:k + 1], row_sum[:, k:k + 1]).then_inc(inv_ready, 1)
                    eng.wait_ge(inv_ready, g + 1)
                    eng.wait_ge(agg_ready, g + 2)
                    if k % STORE == 0:
                        eng.wait_ge(stored[slot], stores * 16 + 1)
                    eng.scalar_tensor_tensor(o_sb[:, slot, k % STORE], agg[:, :], inv_sum[:, k:k + 1],
                                             x_kept[:, x_slot, t], op0=ALU.mult, op1=ALU.add).then_inc(o_ready, 1)

                def body(it, last):
                    for k in range(K):
                        if k % T in SPLIT_STEPS and not (last and k >= T):
                            slot = (k // T + 1) % 2
                            split_hT(it * BPI + k // T + 1, slot, SPLIT_STEPS.index(k % T), [(slot, 0)])
                        if not (last and k + 2 >= K):
                            mask_scores(it, k + 2)
                        if k % T == 0:
                            eng.wait_ge(x_copied, it * BPI + k // T + 1)
                        finish(it * K + k, k, k // STORE, k // T, k % T, it)
                        if k % T in STATS_STEPS and not last:
                            half = STATS_STEPS.index(k % T)
                            if half == 0:
                                eng.wait_ge(x_loaded, 16 * (it * BPI + k // T + 3))
                            statistics(half)
                        if k % T in MOMENTS_STEPS and not (last and k >= T):
                            moments(it * BPI + k // T + 1, MOMENTS_STEPS.index(k % T))
                        if last and k == K - 2:
                            eng.wait_ge(lanes_turned, 1)
                            eng.tensor_reduce(all_least[:, :], turn[0:1, 0:P], AX_X, ALU.min).then_inc(all_least_ready, 1)
                            eng.wait_ge(all_least_ready, 1)
                            eng.tensor_scalar(flag[:, :], all_least[:, :], FLAG_BELOW, None, ALU.is_lt).then_inc(flag_ready, 1)
                        if k == K - 3:
                            eng.wait_ge(least_ready, it + 1)
                            eng.tensor_tensor(least[:, :], least[:, :], neg_max[:, :], ALU.min).then_inc(least_ready, 1)
                            if last:
                                eng.wait_ge(least_ready, ITERS + 1)
                                eng.tensor_reduce(lane_least[:, :], least[:, :], AX_X, ALU.min).then_inc(lane_least_ready, 1)

                eng.sem_inc(o_ready, 1)
                eng.sem_inc(compared, 1)
                eng.memset(least[:, :], 3.0e38).then_inc(least_ready, 1)
                for half, loaded in enumerate((first_x_loaded, x_loaded)):
                    eng.wait_ge(loaded, 16)
                    statistics(half)
                    moments(0, half)
                eng.wait_ge(a_loaded, 64)
                eng.tensor_scalar(neg_a[:, :], a_col[:, :], -1.0, None, ALU.mult).then_inc(neg_a_ready, 1)
                eng.wait_ge(shift_ready, 2)
                for t in range(HT, T):
                    eng.tensor_scalar(h_sb[:, 0, t], x_in[:, t], rstd[:, t:t + 1], shift[:, t:t + 1],
                                      ALU.mult, ALU.add).then_inc(first_scaled, 1)
                eng.wait_ge(first_scaled, HT)
                eng.tensor_scalar(h_sb[:, 0, HT:T], h_sb[:, 0, HT:T], 0.0, None, ALU.max).then_inc(second_half_ready, 1)
                eng.wait_ge(neg_a_ready, 1)
                for half in range(2):
                    split_hT(0, 0, half, [(0, 0)], FIRST_TURN[half])
                mask_scores(0, 0)
                mask_scores(0, 1)
                eng.wait_ge(x_loaded, 32)
                for half in range(2):
                    statistics(half)
                with eng.Fori(0, ITERS - 1) as it:
                    body(it, False)
                body(ITERS - 1, True)

                eng.wait_ge(flag_ready, 1)
                with eng.If(eng.value_load(flag[0:1, 0:1]) != 0):
                    with eng.Fori(0, B) as b:
                        eng.wait_ge(x_loaded, (b + B + 1) * 16)
                        for half in range(2):
                            statistics(half)
                            moments(b + B, half)
                        for half in range(2):
                            split_hT(b + B, 0, half, [(a, a) for a in range(4)])
                        for t in range(T):
                            slot = t // 2 % ADJ_SLOTS
                            eng.wait_ge(adj_loaded[slot], 16 * (b + 1 + B * T // 2 // ADJ_SLOTS))
                            eng.wait_ge(leaky_ready, (b + B) * T + t)
                            eng.memset(masked[:, :], BIG).then_inc(picked0, 1)
                            for a in range(4):
                                if a:
                                    eng.wait_ge(picked, 4 * (b * T + t) + a)
                                eng.tensor_scalar(hit[:, :], adj_sb[:, slot, t % 2], float(a + 1), None,
                                                  ALU.is_equal).then_inc(hit_ready, 1)
                                eng.wait_ge(hit_ready, 4 * (b * T + t) + a + 1)
                                if a == 0:
                                    eng.wait_ge(picked0, b * T + t + 1)
                                if a == 3:
                                    eng.sem_inc(compared, 1)
                                eng.wait_ge(scores_ready, B * T + 4 * (b * T + t) + a + 1)
                                stand_alone(eng)
                                eng.copy_predicated(masked[:, :], hit[:, :], scores[:, a % 2]).then_inc(picked, 1)
                            eng.wait_ge(picked, 4 * (b * T + t) + 4)
                            eng.tensor_reduce(neg_max[:, t:t + 1], masked[:, :], AX_X, ALU.min).then_inc(least_of_row, 1)
                            eng.wait_ge(least_of_row, b * T + t + 1)
                            leaky_relu(b, 0, t)
                            if t == 0:
                                eng.wait_ge(x_copied, b + B + 1)
                            finish((b + B) * T + t, t, t // STORE, 0, t, b + ITERS)


_INS = ["x", "adj", "L0_gnn_a0", "L0_gnn_a1", "L0_gnn_a2", "L0_gnn_a3"]


def kernel(**inputs):
    import numpy as np
    import concourse.bacc as bacc
    from concourse.bass_utils import run_bass_kernel_spmd

    nc = bacc.Bacc("TRN2", target_bir_lowering=False, num_devices=1)
    arrays, args = {}, []
    for name in _INS:
        a = np.ascontiguousarray(inputs[name])
        arrays[f"in_{name}"] = a
        args.append(nc.dram_tensor(f"in_{name}", a.shape, mybir.dt.from_np(a.dtype), kind="ExternalInput").ap())
    shape = inputs["x"].shape
    args.append(nc.dram_tensor("out", shape, F32, kind="ExternalOutput").ap())
    build(nc, *args)
    r = run_bass_kernel_spmd(nc, [arrays], core_ids=[0])
    return r.results[0]["out"]
```
